# Optimizing a Trainium2 kernel written in Bass

```python
import numpy as np
import jax
import jax.numpy as jnp

def _softmax(x, axis=-1):
    return jax.nn.softmax(x, axis=axis)

def _gelu(x):
    return jax.nn.gelu(x, approximate=True)

def _silu(x):
    return jax.nn.silu(x)

def _sigmoid(x):
    return jax.nn.sigmoid(x)

def _layernorm(x, axis=-1, eps=1e-05):
    m = jnp.mean(x, axis=axis, keepdims=True)
    v = jnp.var(x, axis=axis, keepdims=True)
    return (x - m) / jnp.sqrt(v + eps)

def _scatter_add(tgt, idx, src, axis=0):
    return tgt.at[idx].add(src)

def _segment_sum(src, seg, n):
    return jax.ops.segment_sum(src, seg, n)
kernel_name = 'mk_xattn_ffn_d1_seqx_r4_939086'

def setup_inputs(seed: int=0):
    np.random.seed(seed)
    _w = jnp.asarray

    def _rec_inputs():
        import jax
        import jax.numpy as jnp
        _rk = jax.random.key(seed)
        x = -0.0002928 + 1 * jax.random.normal(jax.random.fold_in(_rk, 1), (16, 128, 256), jnp.float32)
        _lenS = 128 - jax.random.randint(jax.random.fold_in(_rk, 7), (16,), 0, max(1, 128 // 4) + 1, jnp.int32)
        _lenS2 = 128 - jax.random.randint(jax.random.fold_in(_rk, 8), (16,), 0, max(1, 128 // 4) + 1, jnp.int32)
        _ctx_1024P = jax.random.normal(jax.random.fold_in(_rk, 11), (16, 16, 256), jnp.float32)
        _ctx_1024c = jax.random.dirichlet(jax.random.fold_in(_rk, 511), 0.3 * jnp.ones((16,), jnp.float32), (16, 128))
        _ctx_1024t = jnp.einsum('bsk,bkd->bsd', _ctx_1024c, _ctx_1024P)
        _ctx_1024t = _ctx_1024t * jax.lax.rsqrt(jnp.mean(jnp.square(_ctx_1024t)) + 1e-12) * 0.953939
        ctx_1024 = -1.39393e-06 + 0.999914 * (_ctx_1024t + 0.3 * jax.random.normal(jax.random.fold_in(_rk, 611), (16, 128, 256), jnp.float32))
        return (x, ctx_1024)
    x, ctx_1024 = _rec_inputs()

    def _L0_xattn_setup():
        import jax, jax.numpy as jnp
        import numpy as np
        D_MODEL = 256
        N_HEAD = 16
        D_HEAD = D_MODEL // N_HEAD
        key = jax.random.key(seed)
        ks = jax.random.split(key, 6)
        B, L, M = (2, 512, 512)
        q = jax.random.normal(ks[0], (B, L, D_MODEL), dtype=jnp.float32)
        kv = jax.random.normal(ks[1], (B, L, D_MODEL), dtype=jnp.float32)
        mem = jax.random.normal(ks[2], (B, M, D_MODEL), dtype=jnp.float32)
        s = 1.0 / np.sqrt(D_MODEL)
        w_q = jax.random.normal(ks[3], (D_MODEL, D_MODEL), dtype=jnp.float32) * s
        w_kv = jax.random.normal(ks[4], (D_MODEL, 2 * D_HEAD), dtype=jnp.float32) * s
        w_concat = jax.random.normal(ks[5], (D_MODEL, D_MODEL), dtype=jnp.float32) * s
        return {'q': q, 'kv': kv, 'mem': mem, 'w_q': w_q, 'w_kv': w_kv, 'w_concat': w_concat}
    _L0_xattn_all = _L0_xattn_setup()
    _L0_xattn_in = {k: v for k, v in _L0_xattn_all.items() if k in ('w_q', 'w_kv', 'w_concat')}
    del _L0_xattn_all

    def _L0_ffn_setup():
        import math
        import jax, jax.numpy as jnp
        import numpy as np
        HIDDEN = 256
        INTER = 1024
        EXPERTS = 8
        B, T = (4, 512)
        EPS = 1e-12
        CAP_FACTOR = 1.0
        MIN_CAP = 4

        def layer_norm(x, g, b, eps=EPS):
            m = jnp.mean(x, axis=-1, keepdims=True)
            v = jnp.var(x, axis=-1, keepdims=True)
            return (x - m) * jax.lax.rsqrt(v + eps) * g + b

        def top1_gate(x, wg, capacity):
            logits = x @ wg
            gates = jax.nn.softmax(logits, axis=-1)
            E = wg.shape[-1]
            idx = jnp.argmax(gates, axis=-1)
            mask1 = jax.nn.one_hot(idx, E, dtype=gates.dtype)
            locations = jnp.cumsum(mask1, axis=0) - mask1
            mask1 = mask1 * (locations < capacity).astype(gates.dtype)
            gates1_s = jnp.sum(gates * mask1, axis=-1)
            loc_s = jnp.sum(locations * mask1, axis=-1).astype(jnp.int32)
            loc_oh = jax.nn.one_hot(loc_s, capacity, dtype=gates.dtype)
            combine = gates1_s[:, None, None] * mask1[:, :, None] * loc_oh[:, None, :]
            dispatch = jax.lax.stop_gradient((combine > 0).astype(x.dtype))
            return (combine, dispatch)
        key = jax.random.key(seed)
        ks = jax.random.split(key, 8)
        s = 0.02
        return {'x': jax.random.normal(ks[0], (B, T, HIDDEN), jnp.float32), 'attn_nw': jnp.ones((HIDDEN,), jnp.float32), 'attn_nb': jnp.zeros((HIDDEN,), jnp.float32), 'wg': jax.random.normal(ks[1], (HIDDEN, EXPERTS), jnp.float32) * s, 'inter_w': jax.random.normal(ks[2], (EXPERTS, HIDDEN, INTER), jnp.float32) * s, 'inter_b': jnp.zeros((EXPERTS, INTER), jnp.float32), 'output_w': jax.random.normal(ks[3], (EXPERTS, INTER, HIDDEN), jnp.float32) * s, 'output_b': jnp.zeros((EXPERTS, HIDDEN), jnp.float32), 'res_inter_w': jax.random.normal(ks[4], (HIDDEN, INTER), jnp.float32) * s, 'res_inter_b': jnp.zeros((INTER,), jnp.float32), 'res_output_w': jax.random.normal(ks[5], (INTER, HIDDEN), jnp.float32) * s, 'res_output_b': jnp.zeros((HIDDEN,), jnp.float32), 'res_coef': jax.random.normal(ks[6], (HIDDEN, 2), jnp.float32) * s}
    _L0_ffn_all = _L0_ffn_setup()
    _L0_ffn_in = {k: v for k, v in _L0_ffn_all.items() if k in ('attn_nw', 'attn_nb', 'wg', 'inter_w', 'inter_b', 'output_w', 'output_b', 'res_inter_w', 'res_inter_b', 'res_output_w', 'res_output_b', 'res_coef')}
    del _L0_ffn_all
    return {'x': x, 'ctx_1024': ctx_1024, 'L0_xattn_w_q': _L0_xattn_in['w_q'], 'L0_xattn_w_kv': _L0_xattn_in['w_kv'], 'L0_xattn_w_concat': _L0_xattn_in['w_concat'], 'L0_ffn_attn_nw': _L0_ffn_in['attn_nw'], 'L0_ffn_attn_nb': _L0_ffn_in['attn_nb'], 'L0_ffn_wg': _L0_ffn_in['wg'], 'L0_ffn_inter_w': _L0_ffn_in['inter_w'], 'L0_ffn_inter_b': _L0_ffn_in['inter_b'], 'L0_ffn_output_w': _L0_ffn_in['output_w'], 'L0_ffn_output_b': _L0_ffn_in['output_b'], 'L0_ffn_res_inter_w': _L0_ffn_in['res_inter_w'], 'L0_ffn_res_inter_b': _L0_ffn_in['res_inter_b'], 'L0_ffn_res_output_w': _L0_ffn_in['res_output_w'], 'L0_ffn_res_output_b': _L0_ffn_in['res_output_b'], 'L0_ffn_res_coef': _L0_ffn_in['res_coef']}

def reference(x, ctx_1024, L0_xattn_w_q, L0_xattn_w_kv, L0_xattn_w_concat, L0_ffn_attn_nw, L0_ffn_attn_nb, L0_ffn_wg, L0_ffn_inter_w, L0_ffn_inter_b, L0_ffn_output_w, L0_ffn_output_b, L0_ffn_res_inter_w, L0_ffn_res_inter_b, L0_ffn_res_output_w, L0_ffn_res_output_b, L0_ffn_res_coef):
    import jax
    import jax.numpy as jnp

    def _L0_xattn_ref(q, kv, mem, w_q, w_kv, w_concat):
        import jax, jax.numpy as jnp
        import numpy as np
        D_MODEL = 256
        N_HEAD = 16
        D_HEAD = D_MODEL // N_HEAD
        B, L, D = q.shape
        c = jnp.concatenate([mem, kv], axis=1)
        qh = (q @ w_q).reshape(B, L, N_HEAD, D_HEAD).transpose(0, 2, 1, 3)
        kvp = c @ w_kv
        k, v = (kvp[..., :D_HEAD], kvp[..., D_HEAD:])
        attn_score = jnp.einsum('bhid,bjd->bhij', qh, k) / np.sqrt(D_HEAD)
        attn_prob = jax.nn.softmax(attn_score, axis=-1)
        out = jnp.einsum('bhij,bjd->bhid', attn_prob, v)
        out = out.transpose(0, 2, 1, 3).reshape(B, L, D)
        return out @ w_concat

    def _L0_ffn_ref(x, attn_nw, attn_nb, wg, inter_w, inter_b, output_w, output_b, res_inter_w, res_inter_b, res_output_w, res_output_b, res_coef):
        import math
        import jax, jax.numpy as jnp
        import numpy as np
        HIDDEN = 256
        INTER = 1024
        EXPERTS = 8
        B, T = (4, 512)
        EPS = 1e-12
        CAP_FACTOR = 1.0
        MIN_CAP = 4

        def layer_norm(x, g, b, eps=EPS):
            m = jnp.mean(x, axis=-1, keepdims=True)
            v = jnp.var(x, axis=-1, keepdims=True)
            return (x - m) * jax.lax.rsqrt(v + eps) * g + b

        def top1_gate(x, wg, capacity):
            logits = x @ wg
            gates = jax.nn.softmax(logits, axis=-1)
            E = wg.shape[-1]
            idx = jnp.argmax(gates, axis=-1)
            mask1 = jax.nn.one_hot(idx, E, dtype=gates.dtype)
            locations = jnp.cumsum(mask1, axis=0) - mask1
            mask1 = mask1 * (locations < capacity).astype(gates.dtype)
            gates1_s = jnp.sum(gates * mask1, axis=-1)
            loc_s = jnp.sum(locations * mask1, axis=-1).astype(jnp.int32)
            loc_oh = jax.nn.one_hot(loc_s, capacity, dtype=gates.dtype)
            combine = gates1_s[:, None, None] * mask1[:, :, None] * loc_oh[:, None, :]
            dispatch = jax.lax.stop_gradient((combine > 0).astype(x.dtype))
            return (combine, dispatch)
        Bx, Tx, M = x.shape
        S = Bx * Tx
        E = wg.shape[-1]
        capacity = max(MIN_CAP, math.ceil(S / E * CAP_FACTOR))
        residual = x.reshape(S, M)
        attn_out = layer_norm(residual, attn_nw, attn_nb)
        combine, dispatch = top1_gate(attn_out, wg, capacity)
        dispatched = jnp.einsum('sec,sm->ecm', dispatch, attn_out)
        h = jax.nn.gelu(jnp.einsum('ecm,emi->eci', dispatched, inter_w) + inter_b[:, None, :], approximate=True)
        expert_out = jnp.einsum('eci,eim->ecm', h, output_w) + output_b[:, None, :]
        moe_out = jnp.einsum('sec,ecm->sm', combine, expert_out)
        rh = jax.nn.gelu(attn_out @ res_inter_w + res_inter_b, approximate=True)
        res_mlp_out = rh @ res_output_w + res_output_b
        coef = jax.nn.softmax(attn_out @ res_coef, axis=-1)
        out = res_mlp_out * coef[:, :1] + moe_out * coef[:, 1:]
        out = out + residual
        return out.reshape(Bx, Tx, M)
    x = x + _L0_xattn_ref(_layernorm(x, axis=-1), ctx_1024, ctx_1024, L0_xattn_w_q, L0_xattn_w_kv, L0_xattn_w_concat)
    x = x + _L0_ffn_ref(_layernorm(x, axis=-1), L0_ffn_attn_nw, L0_ffn_attn_nb, L0_ffn_wg, L0_ffn_inter_w, L0_ffn_inter_b, L0_ffn_output_w, L0_ffn_output_b, L0_ffn_res_inter_w, L0_ffn_res_inter_b, L0_ffn_res_output_w, L0_ffn_res_output_b, L0_ffn_res_coef)
    return x

_drawn_inputs = setup_inputs


def setup_inputs(seed=0):
    import zlib

    import numpy as np

    out = dict(_drawn_inputs(seed))
    spreads = {'L0_ffn_attn_nw': (1.0, 0.6),
     'L0_ffn_attn_nb': (0.0, 0.8),
     'L0_ffn_inter_b': (0.0, 0.8),
     'L0_ffn_output_b': (0.0, 0.8),
     'L0_ffn_res_inter_b': (0.0, 0.8),
     'L0_ffn_res_output_b': (0.0, 0.96)}
    factors = {'L0_ffn_wg': 8.0,
     'L0_ffn_inter_w': 8.0,
     'L0_ffn_output_w': 8.0,
     'L0_ffn_res_coef': 6.85,
     'L0_ffn_res_inter_w': 2.911}
    for name, (base, spread) in spreads.items():
        noise = np.random.default_rng([zlib.crc32(name.encode()), seed]).standard_normal(out[name].shape)
        drawn = base * np.exp(spread * noise) if base else spread * noise
        out[name] = jnp.asarray(drawn.astype(out[name].dtype))
    for name, factor in factors.items():
        out[name] = (out[name] * factor).astype(out[name].dtype)
    return out
```

```python
import concourse.bass as bass
from concourse import mybir
from contextlib import ExitStack


def xattn_moe_ffn_kernel(nc, x, ctx, w_q, w_kv, w_c, nw, nb, wg, inter_w, inter_b, output_w, output_b,
                         res_inter_w, res_inter_b, res_output_w, res_output_b, res_coef, out):
    f32 = mybir.dt.float32
    f32r = mybir.dt.float32r
    bf16 = mybir.dt.bfloat16
    f16 = mybir.dt.float16
    u32 = mybir.dt.uint32
    ALU = mybir.AluOpType
    ACT = mybir.ActivationFunctionType
    AX = mybir.AxisListType.X

    P = 128
    NBATCH, L, D = x.shape
    S = NBATCH * L
    DH = w_kv.shape[1] // 2
    NH = D // DH
    E, _, F = inter_w.shape
    KC = D // P
    FC = F // P
    T = 2
    UT = T * P
    U = S // UT
    CAP = -(-S // E)
    assert CAP == UT and L == P and KC == 2
    N = U + E
    REP = 6
    QPART = (0, 0, 0, 1, 1, 2)
    KPART = (0, 1, 2, 0, 1, 0)
    KS = REP * DH
    VW = 3 * DH + 1
    NG = E + 2
    SCALE = float(DH) ** -0.5
    ROW = D + 2
    R_RES, R_NW, R_NB = E * FC, E * FC + FC, E * FC + FC + KC
    NVEC = R_NB + KC

    x_v = x.rearrange("(u t) p d -> u p t d", t=T)
    ctx_v = ctx.rearrange("(u t) p d -> u p t d", t=T)
    out_v = out.rearrange("(b p) d -> b p d", p=P)

    dram_q = nc.dram_tensor("dram_q", [2, 3, D, UT], bf16).ap()
    disp = nc.dram_tensor("dispatched", [E * CAP + S, ROW], f32).ap()

    plan = [("small", 0), ("ln1", 0), ("wload", 0)]

    def front(u):
        return [("xn", u), ("tr", u), ("qkv", u), ("vt", u), ("stack", u)]

    def scores(u):
        return [("A", u, 0), ("A", u, 1), ("M", u)]

    def back(u):
        return [("B", u, 0), ("B", u, 1), ("PV", u, 0), ("PV", u, 1), ("oT", u), ("proj", u), ("ln2", u)]

    def gate(u):
        return [("cT", u), ("lg", u), ("lgT", u), ("loc", u)]

    def mlp(n):
        return [("up", n, c) for c in range(FC // 2)]

    def down(n):
        return [("down", n, t) for t in range(T)]

    def split(j):
        return [("wsplit", j)] + ([("wload", j + 1)] if j + 1 < 2 * E + 2 else [])

    def merge(main, extra):
        merged, done = [], 0
        for i, step in enumerate(main):
            merged.append(step)
            upto = (i + 1) * len(extra) // len(main)
            merged += extra[done:upto]
            done = upto
        return merged

    plan += front(0) + [("ln1", 1)] + scores(0) + front(1) + split(0) + split(1)
    for u in range(U):
        attention = back(u)
        if u + 1 < U:
            attention += scores(u + 1)
        attention += gate(u)
        if u + 2 < U:
            attention += front(u + 2)
        plan += merge(attention, (mlp(u - 1) if u >= 1 else []) + (down(u - 2) if u >= 2 else []))
    plan += split(2)
    for n in range(U - 1, N):
        if n >= U:
            plan += [("ein", n - U)]
        plan += merge(mlp(n), down(n - 1))
        if n - U + 1 < E:
            j = 2 * (n - U + 1) + 2
            plan += (split(j) if j > 2 else []) + split(j + 1)
    plan += down(N - 1)
    plan += [("end", 0)]

    with ExitStack() as ex:
        def sb(name, shape, dt, stack=ex):
            return stack.enter_context(nc.sbuf_tensor(name, shape, dt))

        ident = sb("ident", [P, P], f32)
        tri = sb("tri", [P, P], bf16)
        ones = sb("ones", [P, P], bf16)
        past = sb("past", [P, NBATCH], f32)
        tokid = sb("tokid", [P, NBATCH], f32)
        desc = sb("desc", [P, T, E], f32)
        zrow = sb("zrow", [P, 2 * T, ROW], f32)
        mhalf = sb("mhalf", [P, NBATCH], f32)
        vrow = sb("vrow", [NVEC, P], f32)
        vecT = sb("vecT", [P, NVEC], f32)
        resb = sb("resb", [P, D], f32)
        outb = sb("outb", [P, 2, D], f32)
        xs = sb("xs", [P, NBATCH, D], f32)
        mv1 = sb("mv1", [P, NBATCH, 2], f32)
        rs1 = sb("rs1", [P, NBATCH], f32)
        mv2 = sb("mv2", [P, NBATCH, 2], f32)
        stats = sb("stats", [P, NBATCH, 6], f32)
        va1 = sb("va1", [P, NBATCH], f32)
        va2 = sb("va2", [P, NBATCH], f32)
        y1 = sb("y1", [P, NBATCH], f32)
        ysq = sb("ysq", [P, NBATCH], f32)
        vr2 = sb("vr2", [P, NBATCH], f32)
        y2 = sb("y2", [P, NBATCH], f32)
        cscale = sb("cscale", [P, NBATCH], f32)
        oneplus = sb("oneplus", [P, NBATCH], f32)
        mrs = sb("mrs", [P, NBATCH], f32)
        coef0 = sb("coef0", [P, NBATCH], f32)
        slot = sb("slot", [P, NBATCH], u32)
        core = sb("core", [P, 2, T, ROW], f32)
        t32 = sb("t32", [P, KC, UT], f32)
        xin_hi = sb("xin_hi", [P, 2, KC, UT], f32r)
        xin_lo = sb("xin_lo", [P, 2, KC, UT], f32r)
        h32 = sb("h32", [P, 2, 2, UT], f32)
        h_hi = sb("h_hi", [P, 2, FC, UT], f32r)
        h_lo = sb("h_lo", [P, 2, FC, UT], f32r)
        dtmp = sb("dtmp", [P, 2, D], f32)
        raw = sb("raw", [P, 2048], f32)
        w1r_hi = sb("w1r_hi", [P, KC, F], f32r)
        w1r_lo = sb("w1r_lo", [P, KC, F], f32r)
        w2r_hi = sb("w2r_hi", [P, FC, D], f32r)
        w2r_lo = sb("w2r_lo", [P, FC, D], f32r)
        wg_raw = sb("wg_raw", [P, KC, NG], f32)
        wg_hi = sb("wg_hi", [P, KC, NG], f32r)
        wg_lo = sb("wg_lo", [P, KC, NG], f32r)
        lgs = sb("lgs", [NG, UT], f32)
        gmax = sb("gmax", [P, T, 2], f32)
        gd = sb("gd", [P, T, NG], f32)
        ge = sb("ge", [P, T, NG], f32)
        gkey = sb("gkey", [P, T, E], f32)
        gkm = sb("gkm", [P, T], f32)
        onehot = sb("onehot", [P, T, E], bf16)
        before = sb("before", [P, T, E], bf16)
        running = sb("running", [P, E], bf16)
        gsum = sb("gsum", [P, T, 2], f32)
        grec = sb("grec", [P, T, 2], f32)
        gbase = sb("gbase", [P, T], f32)
        gloc = sb("gloc", [P, T, E], f32)
        gl = sb("gl", [P, T], f32)
        gkeep = sb("gkeep", [P, T], f32)
        gs0 = sb("gs0", [P, T], f32)
        gs1 = sb("gs1", [P, T], f32)
        gw = sb("gw", [P, T], f32)

        att = ex.enter_context(ExitStack())
        ctxs = sb("ctxs", [P, T, D], f32, att)
        xn = sb("xn", [P, T, D], f32, att)
        cT_hi = sb("cT_hi", [P, KC, UT], f32r, att)
        cT_lo = sb("cT_lo", [P, KC, UT], f32r, att)
        xT_hi = sb("xT_hi", [P, KC, UT], f32r, att)
        xT_lo = sb("xT_lo", [P, KC, UT], f32r, att)
        wq_raw = sb("wq_raw", [P, KC, D], f32, att)
        wq_hi = sb("wq_hi", [P, KC, D], f32r, att)
        wq_lo = sb("wq_lo", [P, KC, D], f32r, att)
        wkv_raw = sb("wkv_raw", [P, KC, 64], f32, att)
        wkv_hi = sb("wkv_hi", [P, KC, 64], f32r, att)
        wkv_lo = sb("wkv_lo", [P, KC, 64], f32r, att)
        wc_raw = sb("wc_raw", [P, KC, D], f32, att)
        wc_hi = sb("wc_hi", [P, KC, D], f32r, att)
        wc_lo = sb("wc_lo", [P, KC, D], f32r, att)
        qres = sb("qres", [P, KC, UT], f32, att)
        qpart = sb("qpart", [P, 3, KC, UT], bf16, att)
        kres = sb("kres", [DH, UT], f32, att)
        kpart = sb("kpart", [DH, 3, UT], bf16, att)
        vT = sb("vT", [64, UT], f32, att)
        vres = sb("vres", [P, T, DH], f32, att)
        vparts = sb("vparts", [P, 2, T, VW], bf16, att)
        qstack = sb("qstack", [KS + 2, 2, NH, UT], bf16, att)
        kstack = sb("kstack", [KS + 2, 2, UT], bf16, att)
        smax = sb("smax", [P, T * NH], f32, att)
        nmax = sb("nmax", [T * NH, 2, P], bf16, att)
        p_hi = sb("p_hi", [P, 2, NH, P], f16, att)
        p_lo = sb("p_lo", [P, 2, NH, P], f16, att)
        p32 = sb("p32", [P, 2, 4, P], f32, att)
        o_sum = sb("o_sum", [P, NH, DH], f32, att)
        o_rec = sb("o_rec", [P, NH], f32, att)
        o_rows = sb("o_rows", [P, T, D], f32, att)
        oT_hi = sb("oT_hi", [P, KC, UT], f32r, att)
        oT_lo = sb("oT_lo", [P, KC, UT], f32r, att)
        att.close()
        w1e_hi = sb("w1e_hi", [P, KC, F], f32r)
        w1e_lo = sb("w1e_lo", [P, KC, F], f32r)
        w2e_hi = sb("w2e_hi", [P, FC, D], f32r)
        w2e_lo = sb("w2e_lo", [P, FC, D], f32r)
        drow = sb("drow", [P, 2, T, ROW], f32)
        rowid = sb("rowid", [P, 2, T], u32)
        accg = sb("accg", [P, 2, T, D], f32)
        yrow = sb("yrow", [P, 2, D], f32)
        W1 = [(w1r_hi, w1r_lo), (w1e_hi, w1e_lo)]
        W2 = [(w2r_hi, w2r_lo), (w2e_hi, w2e_lo)]

        def wset(n):
            return 0 if n < U else (n - U + 1) % 2

        bank = [ex.enter_context(nc.psum_tensor(f"bank{i}", [P, 512], f32)) for i in range(4)]
        pv = ex.enter_context(nc.psum_tensor("pv", [P, NH, 64], f32))
        ubank = [ex.enter_context(nc.psum_tensor(f"ubank{i}", [P, 2, UT], f32)) for i in range(2)]
        mbank, sbank = bank[0:2], bank[2:4]

        sems = {}

        def sem(name):
            if name not in sems:
                sems[name] = ex.enter_context(nc.semaphore(name))
            return sems[name]

        FREED = {
            "vec": ("vec_ready", lambda *k: 1),
            "ctxT": ("ctx_split", lambda u: u + 1), "xT": ("x_split", lambda u: u + 1),
            "q": ("q_resid", lambda u: u + 1), "kv": ("kv_resid", lambda u: u + 1),
            "v": ("v_resid", lambda u: u + 1), "M": ("m_split", lambda u: u + 1),
            "oT": ("oT_split", lambda u: u + 1), "proj": ("x1_ready", lambda u: u + 1),
            "cT": ("ao_t", lambda n: n + 1), "lg": ("lg_copied", lambda u: u + 1),
            "lgT": ("gate_read", lambda u: u + 1), "loc": ("loc_read", lambda u: u + 1),
            "down": ("down_read", lambda n, t: T * n + t + 1),
        }
        USES = {"small": ["vec"], "tr": ["ctxT", "xT"], "qkv": ["q", "kv"], "vt": ["v"], "M": ["M"], "oT": ["oT"],
                "proj": ["proj"], "cT": ["cT"], "lg": ["lg"], "lgT": ["lgT"], "loc": ["loc"], "down": ["down"],
                "ein": ["cT"]}
        place, before_it = {}, {}
        held = []
        for step in plan:
            for use in USES.get(step[0], []):
                key = (use,) + (step[1:] if step[0] != "ein" else (U + step[1],))
                place[key] = len(held) % 2
                before_it[key] = held[-2] if len(held) >= 2 else None
                held.append(key)

        block = ex.enter_context(nc.Block())

        @block.sync
        def _(sp):
            def small(_):
                sp.dma_start(xs[:, 0:T, :], x_v[0]).then_inc(sem("x_in0"), 16)
                sp.dma_start(ctxs[:, :, :], ctx_v[0]).then_inc(sem("ctx_in"), 16)
                sp.dma_start(wq_raw[:, :, :], w_q.rearrange("(k p) n -> p k n", p=P)).then_inc(sem("small_in"), 16)
                for part in range(2):
                    sp.dma_start(wkv_raw[:, :, 32 * part:32 * part + DH],
                                 w_kv[:, part * DH:(part + 1) * DH].rearrange("(k p) n -> p k n", p=P))\
                      .then_inc(sem("small_in"), 16)
                sp.dma_start(wg_raw[:, :, 0:E], wg.rearrange("(k p) n -> p k n", p=P)).then_inc(sem("small_in"), 16)
                sp.dma_start(wg_raw[:, :, E:NG], res_coef.rearrange("(k p) n -> p k n", p=P))\
                  .then_inc(sem("small_in"), 16)
                sp.dma_start(wc_raw[:, :, :], w_c.rearrange("(k p) n -> p k n", p=P)).then_inc(sem("small_in"), 16)
                sp.dma_start(vrow[0:R_RES, :], inter_b.rearrange("e (c p) -> (e c) p", p=P)).then_inc(sem("vec_in"), 16)
                sp.dma_start(vrow[R_RES:R_NW, :], res_inter_b.rearrange("(c p) -> c p", p=P))\
                  .then_inc(sem("vec_in"), 16)
                sp.dma_start(vrow[R_NW:R_NB, :], nw.rearrange("(c p) -> c p", p=P)).then_inc(sem("vec_in"), 16)
                sp.dma_start(vrow[R_NB:NVEC, :], nb.rearrange("(c p) -> c p", p=P)).then_inc(sem("vec_in"), 16)
                for u in range(1, U):
                    sp.dma_start(xs[:, T * u:T * u + T, :], x_v[u]).then_inc(sem("x_in1"), 16)
                sp.dma_start(resb[:, :], res_output_b.partition_broadcast(P)).then_inc(sem("resb_in"), 16)
                sp.wait_ge(sem("zrow_ready"), 3)
                for b in range(E // 2):
                    sp.dma_start(disp[b * 2 * CAP:(b + 1) * 2 * CAP, :].rearrange("(t p) d -> p t d", p=P),
                                 zrow[:, :, :]).then_inc(sem("disp_zero"), 16)
                sp.dma_start(out[S:S + 2 * CAP, :].rearrange("(t p) d -> p t d", p=P), zrow[:, :, 0:D])\
                  .then_inc(sem("acc_out"), 16)

            def ctx_load(u):
                sp.wait_ge(sem("ctxT_done"), u)
                sp.dma_start(ctxs[:, :, :], ctx_v[u]).then_inc(sem("ctx_in"), 16)

            def wload(j):
                if j >= 1:
                    sp.wait_ge(sem("w_lo"), j)
                e = j // 2 - 1
                src1 = res_inter_w if j < 2 else inter_w[e]
                src2 = res_output_w if j < 2 else output_w[e]
                if j % 2 == 0:
                    sp.dma_start(raw[:, :].rearrange("p (k f) -> p k f", k=KC),
                                 src1.rearrange("(k p) f -> p k f", p=P)).then_inc(sem("raw_in"), 16)
                else:
                    sp.dma_start(raw[:, :].rearrange("p (c d) -> p c d", c=FC),
                                 src2.rearrange("(c p) d -> p c d", p=P)).then_inc(sem("raw_in"), 16)

            def stack(u):
                r = u % 2
                sp.wait_ge(sem("q_parts"), u + 1)
                if u >= 2:
                    sp.wait_ge(sem(f"stack_in{r}"), 12 * 16 * (u // 2))
                sp.dma_start(dram_q[r].rearrange("a (m p) t -> p a m t", p=P), qpart[:, :, :, :])\
                  .then_inc(sem("q_spill"), 16)
                sp.wait_ge(sem("k_parts"), u + 1)
                if u >= 2:
                    sp.wait_ge(sem("b_done"), 8 * (u - 1))
                for i, part in enumerate(KPART):
                    sp.dma_start(kstack[i * DH:(i + 1) * DH, r, :], kpart[:, part, :])\
                      .then_inc(sem(f"stack_in{r}"), 16)
                sp.wait_ge(sem("q_spill"), 16 * (u + 1))
                for i, part in enumerate(QPART):
                    sp.dma_start(qstack[i * DH:(i + 1) * DH, r, :, :],
                                 dram_q[r, part].rearrange("(h d) t -> d h t", d=DH))\
                      .then_inc(sem(f"stack_in{r}"), 16)

            def maxima(u):
                sp.wait_ge(sem("m_split"), u + 1)
                for b in range(T):
                    for part in range(2):
                        sp.dma_start(qstack[KS + part:KS + part + 1, u % 2, :, b * P:(b + 1) * P],
                                     nmax[b * NH:(b + 1) * NH, part, :]).then_inc(sem(f"m_in{u % 2}"), 16)

            def expert_in(e):
                if e == 0:
                    for r in range(2):
                        sp.wait_ge(sem(f"disp_in{r}"), 16 * T * U // 2)
                if e >= 2:
                    sp.wait_ge(sem("down_read"), T * (U + e - 1))
                sp.dma_start(outb[:, e % 2, :], output_b[e].partition_broadcast(P)).then_inc(sem(f"outb_in{e % 2}"), 16)
                sp.dma_start(drow[:, e % 2, :, :], disp[e * CAP:(e + 1) * CAP, :].rearrange("(t p) d -> p t d", p=P))\
                  .then_inc(sem(f"drow_in{e % 2}"), 16)

            def down(n, t):
                if n < U:
                    sp.wait_ge(sem("acc_ready"), T * n + t + 1)
                    sp.dma_start(out_v[T * n + t], xs[:, T * n + t, :]).then_inc(sem("acc_out"), 16)

            def end(_):
                sp.wait_ge(sem("acc_out"), 16 * (NBATCH + 1))

            for step in plan:
                kind, k = step[0], step[1:]
                if kind == "small":
                    small(*k)
                elif kind == "tr" and k[0] >= 1:
                    ctx_load(*k)
                elif kind == "wload":
                    wload(*k)
                elif kind == "stack":
                    stack(*k)
                elif kind == "M":
                    maxima(*k)
                elif kind == "ein":
                    expert_in(*k)
                elif kind == "down":
                    down(*k)
                elif kind == "end":
                    end(*k)

        @block.gpsimd
        def _(pool):
            steps = [0]

            def own(ins):
                steps[0] += 1
                ins.then_inc(sem("pool_step"), 1)
                pool.wait_ge(sem("pool_step"), steps[0])

            def small(_):
                own(pool.memset(ident[:, :], 0.0))
                pool.affine_select(out=ident[:, :], in_=ident[:, :], compare_op=ALU.not_equal, fill=1.0, base=0,
                                   pattern=[[-1, P]], channel_multiplier=1).then_inc(sem("ident_ready"), 1)
                pool.memset(mhalf[:, :], -0.5).then_inc(sem("mhalf_ready"), 1)
                own(pool.memset(tri[:, :], 1.0))
                pool.affine_select(out=tri[:, :], in_=tri[:, :], compare_op=ALU.is_gt, fill=0.0, base=0,
                                   pattern=[[1, P]], channel_multiplier=-1).then_inc(sem("route_const"), 1)
                pool.memset(ones[:, :], 1.0).then_inc(sem("route_const"), 1)
                pool.memset(running[:, :], 0.0).then_inc(sem("route_const"), 1)
                pool.iota(past[:, :], [[P, NBATCH]], base=E * CAP, channel_multiplier=1,
                          allow_small_or_imprecise_dtypes=True).then_inc(sem("route_const"), 1)
                pool.iota(tokid[:, :], [[P, NBATCH]], base=0, channel_multiplier=1,
                          allow_small_or_imprecise_dtypes=True).then_inc(sem("route_const"), 1)
                pool.iota(desc[:, :, :], [[0, T], [-1, E]], base=E, channel_multiplier=0,
                          allow_small_or_imprecise_dtypes=True).then_inc(sem("route_const"), 1)
                pool.memset(zrow[:, :, 0:D], 0.0).then_inc(sem("zrow_ready"), 1)
                pool.iota(zrow[:, :, D], [[P, 2 * T]], base=S, channel_multiplier=1,
                          allow_small_or_imprecise_dtypes=True).then_inc(sem("zrow_ready"), 1)
                pool.memset(zrow[:, :, D + 1], 0.0).then_inc(sem("zrow_ready"), 1)

            def ln1(part):
                a, b = (0, T) if part == 0 else (T, NBATCH)
                pool.wait_ge(sem("mhalf_ready"), 1)
                pool.wait_ge(sem("ln1_var"), part + 1)
                pool.tensor_tensor(rs1[:, a:b], va1[:, a:b], mhalf[:, a:b], ALU.pow).then_inc(sem("ln1_rs"), 1)

            def ln2(u):
                c = slice(T * u, T * u + T)
                pool.wait_ge(sem("ln2_var"), u + 1)
                own(pool.tensor_tensor(y1[:, c], va2[:, c], mhalf[:, c], ALU.pow))
                own(pool.tensor_tensor(ysq[:, c], y1[:, c], y1[:, c], ALU.mult))
                own(pool.tensor_tensor(ysq[:, c], ysq[:, c], mv2[:, c, 1], ALU.mult))
                own(pool.tensor_scalar(vr2[:, c], ysq[:, c], 1e-12, None, ALU.add))
                own(pool.tensor_tensor(y2[:, c], vr2[:, c], mhalf[:, c], ALU.pow))
                pool.tensor_scalar(oneplus[:, c], y1[:, c], 1.0, None, ALU.add).then_inc(sem("ln2_done"), 1)
                pool.tensor_tensor(mrs[:, c], y1[:, c], mv2[:, c, 0], ALU.mult).then_inc(sem("ln2_done"), 1)
                pool.tensor_tensor(cscale[:, c], y1[:, c], y2[:, c], ALU.mult).then_inc(sem("ln2_done"), 1)

            def wsplit(j):
                w = wset(0 if j < 2 else U + j // 2 - 1)
                hi, lo = (W1 if j % 2 == 0 else W2)[w]
                hi = hi[:, :, :].rearrange("p a b -> p (a b)")
                lo = lo[:, :, :].rearrange("p a b -> p (a b)")
                for q in range(4):
                    c = slice(512 * q, 512 * q + 512)
                    pool.wait_ge(sem("w_hi"), 4 * j + q + 1)
                    ins = pool.tensor_tensor(lo[:, c], raw[:, c], hi[:, c].bitcast(f32), ALU.subtract)
                ins.then_inc(sem("w_lo"), 1)

            def scatter(u):
                pool.wait_ge(sem("slot_ready"), u + 1)
                if u == 0:
                    pool.wait_ge(sem("disp_zero"), 16 * (E // 2))
                for t in range(T):
                    i = T * u + t
                    pool.indirect_dma_start(out=disp[:, :], in_=core[:, u % 2, t, :], in_offset=None,
                                            out_offset=bass.IndirectOffsetOnAxis(ap=slot[:, i:i + 1], axis=0))\
                        .then_inc(sem(f"disp_in{u % 2}"), 16)

            def expert_in(e):
                pool.wait_ge(sem("rowid_ready"), e + 1)
                if e == 0:
                    pool.wait_ge(sem("acc_out"), 16 * (NBATCH + 1))
                if e >= 2:
                    pool.wait_ge(sem("y_ready"), T * (e - 1))
                    for t in range(T):
                        pool.wait_ge(sem(f"y_out{t}"), 16 * (e - 1))
                for t in range(T):
                    pool.indirect_dma_start(out=accg[:, e % 2, t, :], in_=out[:, :], out_offset=None,
                                            in_offset=bass.IndirectOffsetOnAxis(ap=rowid[:, e % 2, t:t + 1], axis=0))\
                        .then_inc(sem(f"accg_in{e % 2}"), 16)

            def down(n, t):
                e = n - U
                if e < 0:
                    return
                pool.wait_ge(sem("y_ready"), T * e + t + 1)
                pool.indirect_dma_start(out=out[:, :], in_=yrow[:, t, :], in_offset=None,
                                        out_offset=bass.IndirectOffsetOnAxis(ap=rowid[:, e % 2, t:t + 1], axis=0))\
                    .then_inc(sem(f"y_out{t}"), 16)

            def end(_):
                for t in range(T):
                    pool.wait_ge(sem(f"y_out{t}"), 16 * E)

            for step in plan:
                kind, k = step[0], step[1:]
                if kind == "small":
                    small(*k)
                elif kind == "ln1":
                    ln1(*k)
                elif kind == "ln2":
                    ln2(*k)
                elif kind == "wsplit":
                    wsplit(*k)
                elif kind == "loc":
                    scatter(*k)
                elif kind == "ein":
                    expert_in(*k)
                elif kind == "down":
                    down(*k)
                elif kind == "end":
                    end(*k)

        @block.tensor
        def _(pe):
            def claim(*key):
                held_before = before_it[key]
                if held_before is not None:
                    name, value = FREED[held_before[0]]
                    pe.wait_ge(sem(name), value(*held_before[1:]))
                return mbank[place[key]]

            def transposes(dst, src, done):
                for kc in range(KC):
                    for t in range(T):
                        o = kc * UT + t * P
                        last = nc.tensor.transpose(dst[:, o:o + P], src[:, t, kc * P:(kc + 1) * P], ident[:, :])
                last.then_inc(sem(done), 1)

            def product3(dst, w_hi, w_lo, v_hi, v_lo):
                n = len(w_hi)
                for kc in range(n):
                    nc.tensor.matmul(dst, w_hi[kc], v_hi[kc], start=(kc == 0), stop=False)
                    nc.tensor.matmul(dst, w_hi[kc], v_lo[kc], start=False, stop=False)
                    last = nc.tensor.matmul(dst, w_lo[kc], v_hi[kc], start=False, stop=(kc == n - 1))
                return last

            def chunks(a, cols=slice(None)):
                return [a[:, kc, cols] for kc in range(KC)]

            def small(_):
                pe.wait_ge(sem("ident_ready"), 1)
                pe.wait_ge(sem("vec_in"), 64)
                b = claim("vec", 0)
                nc.tensor.transpose(b[:, 0:NVEC], vrow[0:NVEC, :], ident[0:NVEC, 0:NVEC]).then_inc(sem("vec_done"), 1)

            def tr(u):
                pe.wait_ge(sem("ctx_in"), 16 * (u + 1))
                transposes(claim("ctxT", u), ctxs, "ctxT_done")
                pe.wait_ge(sem("xn_ready"), u + 1)
                transposes(claim("xT", u), xn, "xT_done")

            def qkv(u):
                if u == 0:
                    pe.wait_ge(sem("smallw_lo"), 4)
                b = claim("q", u)
                pe.wait_ge(sem("x_split"), u + 1)
                for m in range(KC):
                    c = slice(m * P, (m + 1) * P)
                    last = product3(b[:, m * UT:(m + 1) * UT], chunks(wq_hi, c), chunks(wq_lo, c),
                                    chunks(xT_hi), chunks(xT_lo))
                last.then_inc(sem("q_done"), 1)
                b = claim("kv", u)
                pe.wait_ge(sem("ctx_split"), u + 1)
                product3(b[0:64, 0:UT], chunks(wkv_hi), chunks(wkv_lo), chunks(cT_hi), chunks(cT_lo))\
                    .then_inc(sem("kv_done"), 1)

            def vt(u):
                b = claim("v", u)
                pe.wait_ge(sem("vT_ready"), u + 1)
                for t in range(T):
                    last = nc.tensor.transpose(b[:, 32 * t:32 * t + 32], vT[32:64, t * P:(t + 1) * P],
                                               ident[32:64, 32:64])
                last.then_inc(sem("v_done"), 1)

            def score_max(u, b):
                r = u % 2
                if b == 0:
                    pe.wait_ge(sem(f"stack_in{r}"), 12 * 16 * (u // 2 + 1))
                for g in range(4):
                    i = 8 * u + 4 * b + g
                    s_free(i, u, "A")
                    for h in range(4):
                        last = nc.tensor.matmul(s_bank(i, u, "A")[:, h * P:(h + 1) * P],
                                                qstack[0:KS, r, 4 * g + h, b * P:(b + 1) * P],
                                                kstack[0:KS, r, b * P:(b + 1) * P], start=True, stop=True)
                    last.then_inc(sem("a_done"), 1)

            def s_bank(i, u, kind):
                return sbank[i % 2]

            def s_free(i, u, kind):
                prev = s_prev[(kind, i)]
                if prev is not None:
                    pe.wait_ge(sem("a_read" if prev[0] == "A" else "b_exp"), prev[1] + 1)

            def max_rows(u):
                b = claim("M", u)
                pe.wait_ge(sem("a_read"), 8 * (u + 1))
                nc.tensor.transpose(b[0:T * NH, 0:P], smax[:, :], ident[:, :]).then_inc(sem("m_done"), 1)

            def scores_T(u, b):
                r = u % 2
                if b == 0:
                    pe.wait_ge(sem(f"m_in{r}"), 4 * 16 * (u // 2 + 1))
                for g in range(4):
                    i = 8 * u + 4 * b + g
                    s_free(i, u, "B")
                    nc.tensor.matmul(s_bank(i, u, "B")[:, :], kstack[:, r, b * P:(b + 1) * P],
                                     qstack[:, r, 4 * g:4 * g + 4, b * P:(b + 1) * P], start=True, stop=True)\
                        .then_inc(sem("b_done"), 1)

            def weigh(u, b):
                i = T * u + b
                pe.wait_ge(sem("v_parts"), u + 1)
                pe.wait_ge(sem("p_lo"), 4 * (i + 1))
                if i >= 1:
                    pe.wait_ge(sem("o_ready"), i)
                for h in range(NH):
                    nc.tensor.matmul(pv[:, h, 0:VW], p_hi[:, i % 2, h, :], vparts[:, u % 2, b, :],
                                     start=True, stop=False)
                    last = nc.tensor.matmul(pv[:, h, 0:VW], p_lo[:, i % 2, h, :], vparts[:, u % 2, b, :],
                                            start=False, stop=True)
                last.then_inc(sem("pv_done"), 1)

            def oT(u):
                b = claim("oT", u)
                pe.wait_ge(sem("o_ready"), T * (u + 1))
                transposes(b, o_rows, "oT_done")

            def proj(u):
                b = claim("proj", u)
                pe.wait_ge(sem("oT_split"), u + 1)
                for t in range(T):
                    c = slice(t * P, (t + 1) * P)
                    last = product3(b[:, t * D:(t + 1) * D], chunks(oT_hi, c), chunks(oT_lo, c),
                                    chunks(wc_hi), chunks(wc_lo))
                last.then_inc(sem("proj_done"), 1)

            def cT(u):
                b = claim("cT", u)
                pe.wait_ge(sem("core_ready"), u + 1)
                transposes(b, core[:, u % 2, :, 0:D], "cT_done")

            def lg(u):
                b = claim("lg", u)
                pe.wait_ge(sem("xin_lo"), u + 1)
                product3(b[0:NG, 0:UT], chunks(wg_hi), chunks(wg_lo), chunks(xin_hi[:, u % 2, :, :]),
                         chunks(xin_lo[:, u % 2, :, :])).then_inc(sem("lg_done"), 1)

            def lgT(u):
                b = claim("lgT", u)
                pe.wait_ge(sem("lg_copied"), u + 1)
                for t in range(T):
                    last = nc.tensor.transpose(b[:, t * NG:(t + 1) * NG], lgs[0:NG, t * P:(t + 1) * P],
                                               ident[0:NG, 0:NG])
                last.then_inc(sem("lgT_done"), 1)

            def loc(u):
                b = claim("loc", u)
                if u == 0:
                    pe.wait_ge(sem("route_const"), 6)
                pe.wait_ge(sem("onehot_ready"), u + 1)
                for t in range(T):
                    o = b[:, t * E:(t + 1) * E]
                    nc.tensor.matmul(o, tri[:, :], onehot[:, t, :], start=True, stop=False)
                    last = nc.tensor.matmul(o, ones[:, :], before[:, t, :], start=False, stop=True)
                last.then_inc(sem("loc_done"), 1)

            def ein(e):
                b = claim("cT", U + e)
                pe.wait_ge(sem(f"drow_in{e % 2}"), 16 * (e // 2 + 1))
                transposes(b, drow[:, e % 2, :, 0:D], "cT_done")

            def up(n, c2):
                i = (FC // 2) * n + c2
                w_hi, w_lo = W1[wset(n)]
                if c2 == 0:
                    pe.wait_ge(sem("xin_lo"), n + 1)
                    pe.wait_ge(sem("w_lo"), 1 if n < U else 2 * (n - U) + 3)
                if i >= 2:
                    pe.wait_ge(sem("gelu_done"), 2 * (i - 1))
                v_hi, v_lo = chunks(xin_hi[:, n % 2, :, :]), chunks(xin_lo[:, n % 2, :, :])
                for j in range(2):
                    c = slice((2 * c2 + j) * P, (2 * c2 + j + 1) * P)
                    last = product3(ubank[i % 2][:, j, :], chunks(w_hi, c), chunks(w_lo, c), v_hi, v_lo)
                last.then_inc(sem("up_done"), 1)

            def down(n, t):
                b = claim("down", n, t)
                w_hi, w_lo = W2[wset(n)]
                if t == 0:
                    pe.wait_ge(sem("h_lo"), (FC // 2) * (n + 1))
                    pe.wait_ge(sem("w_lo"), 2 if n < U else 2 * (n - U) + 4)
                c = slice(t * P, (t + 1) * P)
                product3(b[:, 0:D], [h_hi[:, n % 2, f, c] for f in range(FC)],
                         [h_lo[:, n % 2, f, c] for f in range(FC)],
                         [w_hi[:, f, :] for f in range(FC)], [w_lo[:, f, :] for f in range(FC)])\
                    .then_inc(sem("down_done"), 1)

            s_prev, s_order = {}, []
            for step in plan:
                if step[0] in ("A", "B"):
                    for g in range(4):
                        key = (step[0], 8 * step[1] + 4 * step[2] + g)
                        s_prev[key] = next((k for k in reversed(s_order) if k[1] % 2 == key[1] % 2), None)
                        s_order.append(key)

            calls = {"small": small, "tr": tr, "qkv": qkv, "vt": vt, "A": score_max, "M": max_rows, "B": scores_T,
                     "PV": weigh, "oT": oT, "proj": proj, "cT": cT, "lg": lg, "lgT": lgT, "loc": loc, "ein": ein,
                     "up": up, "down": down}
            for step in plan:
                if step[0] in calls:
                    calls[step[0]](*step[1:])

        @block.scalar
        def _(act):
            def copy(dst, src, scale=1.0):
                return nc.scalar.activation(dst, src, ACT.Copy, scale=scale)

            def small(_):
                act.wait_ge(sem("small_in"), 16 * 6)
                act.wait_ge(sem("wkv_zero"), 1)
                for hi, rw in ((wq_hi, wq_raw), (wkv_hi, wkv_raw), (wc_hi, wc_raw), (wg_hi, wg_raw)):
                    copy(hi[:, :, :], rw[:, :, :]).then_inc(sem("smallw_hi"), 1)

            def tr(u):
                act.wait_ge(sem("ctxT_done"), u + 1)
                if u >= 1:
                    act.wait_ge(sem("kv_done"), u)
                copy(cT_hi[:, :, :], mbank[place[("ctxT", u)]][:, :].rearrange("p (k t) -> p k t", k=KC))\
                    .then_inc(sem("ctx_hi"), 1)
                act.wait_ge(sem("xT_done"), u + 1)
                copy(xT_hi[:, :, :], mbank[place[("xT", u)]][:, :].rearrange("p (k t) -> p k t", k=KC))\
                    .then_inc(sem("x_hi"), 1)

            def qkv(u):
                act.wait_ge(sem("q_done"), u + 1)
                if u >= 1:
                    act.wait_ge(sem("q_spill"), 16 * u)
                copy(qpart[:, 0, :, :], mbank[place[("q", u)]][:, :].rearrange("p (k t) -> p k t", k=KC))\
                    .then_inc(sem("q_hi"), 1)
                act.wait_ge(sem("kv_done"), u + 1)
                if u >= 1:
                    act.wait_ge(sem(f"stack_in{(u - 1) % 2}"), 12 * 16 * ((u - 1) // 2 + 1))
                    act.wait_ge(sem("v_done"), u)
                b = mbank[place[("kv", u)]]
                copy(kpart[:, 0, :], b[0:DH, 0:UT]).then_inc(sem("k_hi"), 1)
                copy(vT[32:64, :], b[32:64, 0:UT]).then_inc(sem("vT_ready"), 1)

            def max_rows(u):
                act.wait_ge(sem("m_done"), u + 1)
                if u >= 1:
                    act.wait_ge(sem(f"m_in{(u - 1) % 2}"), 4 * 16 * ((u - 1) // 2 + 1))
                copy(nmax[:, 0, :], mbank[place[("M", u)]][0:T * NH, 0:P], -1.0).then_inc(sem("m_hi"), 1)

            def scores_T(u, b):
                i = T * u + b
                if i >= 2:
                    act.wait_ge(sem("pv_done"), i - 1)
                for g in range(4):
                    k = 4 * i + g
                    act.wait_ge(sem("b_done"), k + 1)
                    s = sbank[k % 2][:, :].rearrange("p (h t) -> p h t", h=4)
                    nc.scalar.activation(p_hi[:, i % 2, 4 * g:4 * g + 4, :], s, ACT.Exp, scale=SCALE)\
                        .then_inc(sem("p_hi"), 1)
                    if k >= 2:
                        act.wait_ge(sem("p_lo"), k - 1)
                    nc.scalar.activation(p32[:, k % 2, :, :], s, ACT.Exp, scale=SCALE).then_inc(sem("b_exp"), 1)

            def oT(u):
                act.wait_ge(sem("oT_done"), u + 1)
                if u >= 1:
                    act.wait_ge(sem("proj_done"), u)
                copy(oT_hi[:, :, :], mbank[place[("oT", u)]][:, :].rearrange("p (k t) -> p k t", k=KC))\
                    .then_inc(sem("oT_hi"), 1)

            def xin(n):
                act.wait_ge(sem("ao_t"), n + 1)
                if n >= 2:
                    act.wait_ge(sem("up_done"), (FC // 2) * (n - 1))
                    if n - 2 < U:
                        act.wait_ge(sem("lg_done"), n - 1)
                copy(xin_hi[:, n % 2, :, :], t32[:, :, :]).then_inc(sem("xin_hi"), 1)

            def lg(u):
                act.wait_ge(sem("lg_done"), u + 1)
                if u >= 1:
                    act.wait_ge(sem("lgT_done"), u)
                copy(lgs[:, :], mbank[place[("lg", u)]][0:NG, 0:UT]).then_inc(sem("lg_copied"), 1)

            def lgT(u):
                act.wait_ge(sem("gate_read"), u + 1)
                nc.scalar.activation(ge[:, :, :], gd[:, :, :], ACT.Exp).then_inc(sem("gate_exp"), 1)

            def wsplit(j):
                w = wset(0 if j < 2 else U + j // 2 - 1)
                hi = (W1 if j % 2 == 0 else W2)[w][0][:, :, :].rearrange("p a b -> p (a b)")
                act.wait_ge(sem("raw_in"), 16 * (j + 1))
                e = j // 2 - 1
                if e >= 0 and e % 2 == 0 and e < 2:
                    act.wait_ge(sem("lg_done"), U)
                    act.wait_ge(sem("x1_ready"), U)
                if e >= 0:
                    user = U - 1 if e == 1 else U + e - 2
                    if e >= 1:
                        act.wait_ge(sem("up_done"), (FC // 2) * (user + 1))
                        if j % 2 == 1:
                            act.wait_ge(sem("down_done"), T * (user + 1))
                for q in range(4):
                    copy(hi[:, 512 * q:512 * q + 512], raw[:, 512 * q:512 * q + 512]).then_inc(sem("w_hi"), 1)

            def up(n, c2):
                i = (FC // 2) * n + c2
                act.wait_ge(sem("up_done"), i + 1)
                if i >= 2:
                    act.wait_ge(sem("h_lo"), i - 1)
                if i == 0:
                    act.wait_ge(sem("vec_ready"), 1)
                for j in range(2):
                    col = (R_RES if n < U else (n - U) * FC) + 2 * c2 + j
                    nc.scalar.activation(h32[:, i % 2, j, :], ubank[i % 2][:, j, :], ACT.Gelu_apprx_tanh,
                                         bias=vecT[:, col:col + 1]).then_inc(sem("gelu_done"), 1)
                if n >= 2 and c2 == 0:
                    act.wait_ge(sem("down_done"), T * (n - 1))
                act.wait_ge(sem("gelu_done"), 2 * (i + 1))
                copy(h_hi[:, n % 2, 2 * c2:2 * c2 + 2, :], h32[:, i % 2, :, :]).then_inc(sem("h_hi"), 1)

            calls = {"small": small, "tr": tr, "qkv": qkv, "M": max_rows, "B": scores_T, "oT": oT, "cT": xin,
                     "ein": lambda e: xin(U + e), "lg": lg, "lgT": lgT, "wsplit": wsplit, "up": up}
            for step in plan:
                if step[0] in calls:
                    calls[step[0]](*step[1:])

        @block.vector
        def _(dve):
            V = nc.vector
            steps = [0]

            def own(ins):
                steps[0] += 1
                ins.then_inc(sem("dve_step"), 1)
                return steps[0]

            def after(n):
                dve.wait_ge(sem("dve_step"), n)

            def two(bank_):
                return bank_[:, :].rearrange("p (k t) -> p k t", k=KC)

            def small(_):
                V.memset(wkv_raw[:, :, DH:32], 0.0)
                V.memset(wkv_raw[:, :, 32 + DH:64], 0.0).then_inc(sem("wkv_zero"), 1)
                V.memset(vparts[:, :, :, 3 * DH:VW], 1.0).then_inc(sem("ones_ready"), 1)
                V.memset(kstack[KS:KS + 2, :, :], 1.0).then_inc(sem("ones_ready"), 1)
                dve.wait_ge(sem("vec_done"), 1)
                V.tensor_copy(vecT[:, :], mbank[place[("vec", 0)]][:, 0:NVEC]).then_inc(sem("vec_ready"), 1)
                for i, (hi, lo, rw) in enumerate(((wq_hi, wq_lo, wq_raw), (wkv_hi, wkv_lo, wkv_raw),
                                                  (wc_hi, wc_lo, wc_raw), (wg_hi, wg_lo, wg_raw))):
                    dve.wait_ge(sem("smallw_hi"), i + 1)
                    V.tensor_tensor(lo[:, :, :], rw[:, :, :], hi[:, :, :].bitcast(f32), ALU.subtract)\
                        .then_inc(sem("smallw_lo"), 1)

            def ln1(part):
                a, b = (0, T) if part == 0 else (T, NBATCH)
                if part == 0:
                    dve.wait_ge(sem("x_in0"), 16)
                else:
                    dve.wait_ge(sem("x_in1"), 16 * (U - 1))
                for i in range(a, b):
                    n = own(V.bn_stats(stats[:, i, :], xs[:, i, :]))
                after(n)
                for i in range(a, b):
                    n = own(V.bn_aggr(mv1[:, i, :], stats[:, i, :]))
                after(n)
                V.tensor_scalar(va1[:, a:b], mv1[:, a:b, 1], 1e-5, None, ALU.add).then_inc(sem("ln1_var"), 1)

            def norm_x(u):
                dve.wait_ge(sem("ln1_rs"), 1 if u == 0 else 2)
                if u >= 1:
                    dve.wait_ge(sem("xT_done"), u)
                for t in range(T):
                    i = T * u + t
                    ins = V.tensor_scalar(xn[:, t, :], xs[:, i, :], mv1[:, i, 0:1], rs1[:, i:i + 1],
                                          ALU.subtract, ALU.mult)
                ins.then_inc(sem("xn_ready"), 1)

            def tr(u):
                dve.wait_ge(sem("ctx_hi"), u + 1)
                V.tensor_tensor(cT_lo[:, :, :], two(mbank[place[("ctxT", u)]]), cT_hi[:, :, :].bitcast(f32),
                                ALU.subtract).then_inc(sem("ctx_split"), 1)
                dve.wait_ge(sem("x_hi"), u + 1)
                V.tensor_tensor(xT_lo[:, :, :], two(mbank[place[("xT", u)]]), xT_hi[:, :, :].bitcast(f32),
                                ALU.subtract).then_inc(sem("x_split"), 1)

            def qkv(u):
                dve.wait_ge(sem("q_hi"), u + 1)
                V.tensor_tensor(qres[:, :, :], two(mbank[place[("q", u)]]), qpart[:, 0, :, :], ALU.subtract)\
                    .then_inc(sem("q_resid"), 1)
                dve.wait_ge(sem("q_resid"), u + 1)
                n = own(V.tensor_copy(qpart[:, 1, :, :], qres[:, :, :]))
                dve.wait_ge(sem("vT_ready"), u + 1)
                V.tensor_tensor(kres[:, :], mbank[place[("kv", u)]][0:DH, 0:UT], kpart[:, 0, :], ALU.subtract)\
                    .then_inc(sem("kv_resid"), 1)
                after(n)
                V.tensor_tensor(qpart[:, 2, :, :], qres[:, :, :], qpart[:, 1, :, :], ALU.subtract)\
                    .then_inc(sem("q_parts"), 1)
                dve.wait_ge(sem("kv_resid"), u + 1)
                n = own(V.tensor_copy(kpart[:, 1, :], kres[:, :]))
                after(n)
                V.tensor_tensor(kpart[:, 2, :], kres[:, :], kpart[:, 1, :], ALU.subtract).then_inc(sem("k_parts"), 1)

            def vt(u):
                dve.wait_ge(sem("v_done"), u + 1)
                if u >= 2:
                    dve.wait_ge(sem("pv_done"), T * (u - 1))
                s = mbank[place[("v", u)]][:, 0:32 * T].rearrange("p (t d) -> p t d", t=T)[:, :, 0:DH]
                v = vparts[:, u % 2, :, :]
                after(own(V.tensor_copy(v[:, :, 0:DH], s)))
                V.tensor_tensor(vres[:, :, :], s, v[:, :, 0:DH], ALU.subtract).then_inc(sem("v_resid"), 1)
                dve.wait_ge(sem("v_resid"), u + 1)
                after(own(V.tensor_copy(v[:, :, DH:2 * DH], vres[:, :, :])))
                V.tensor_tensor(v[:, :, 2 * DH:3 * DH], vres[:, :, :], v[:, :, DH:2 * DH], ALU.subtract)\
                    .then_inc(sem("v_parts"), 1)

            def score_max(u, b):
                if u >= 1 and b == 0:
                    dve.wait_ge(sem("m_done"), u)
                for g in range(4):
                    i = 8 * u + 4 * b + g
                    dve.wait_ge(sem("a_done"), i + 1)
                    c = b * NH + 4 * g
                    V.reduce_max(smax[:, c:c + 4], sbank[i % 2][:, :].rearrange("p (h t) -> p h t", h=4), AX)\
                        .then_inc(sem("a_read"), 1)

            def max_rows(u):
                dve.wait_ge(sem("m_hi"), u + 1)
                V.scalar_tensor_tensor(out=nmax[:, 1, :], in0=mbank[place[("M", u)]][0:T * NH, 0:P], scalar=-1.0,
                                       in1=nmax[:, 0, :], op0=ALU.mult, op1=ALU.subtract).then_inc(sem("m_split"), 1)

            def scores_T(u, b):
                i = T * u + b
                for g in range(4):
                    k = 4 * i + g
                    dve.wait_ge(sem("b_exp"), k + 1)
                    V.tensor_tensor(p_lo[:, i % 2, 4 * g:4 * g + 4, :], p32[:, k % 2, :, :],
                                    p_hi[:, i % 2, 4 * g:4 * g + 4, :], ALU.subtract).then_inc(sem("p_lo"), 1)

            def weigh(u, b):
                i = T * u + b
                dve.wait_ge(sem("pv_done"), i + 1)
                if u >= 1 and b == 0:
                    dve.wait_ge(sem("oT_done"), u)
                V.reciprocal(o_rec[:, :], pv[:, :, VW - 1])
                n = own(V.tensor_reduce(o_sum[:, :, :], pv[:, :, 0:3 * DH].rearrange("p h (a d) -> p h d a", a=3),
                                        AX, ALU.add))
                after(n)
                V.tensor_tensor(o_rows[:, b, :].rearrange("p (h d) -> p h d", d=DH), o_sum[:, :, :],
                                o_rec[:, :].unsqueeze(2).broadcast_to([P, NH, DH]), ALU.mult)\
                    .then_inc(sem("o_ready"), 1)

            def oT(u):
                dve.wait_ge(sem("oT_hi"), u + 1)
                V.tensor_tensor(oT_lo[:, :, :], two(mbank[place[("oT", u)]]), oT_hi[:, :, :].bitcast(f32),
                                ALU.subtract).then_inc(sem("oT_split"), 1)

            def proj(u):
                c = slice(T * u, T * u + T)
                dve.wait_ge(sem("proj_done"), u + 1)
                V.tensor_tensor(xs[:, c, :], xs[:, c, :], mbank[place[("proj", u)]][:, :]
                                .rearrange("p (t d) -> p t d", t=T), ALU.add).then_inc(sem("x1_ready"), 1)

            def ln2(u):
                c = slice(T * u, T * u + T)
                dve.wait_ge(sem("x1_ready"), u + 1)
                for i in range(T * u, T * u + T):
                    n = own(V.bn_stats(stats[:, i, :], xs[:, i, :]))
                after(n)
                for i in range(T * u, T * u + T):
                    n = own(V.bn_aggr(mv2[:, i, :], stats[:, i, :]))
                after(n)
                V.tensor_scalar(va2[:, c], mv2[:, c, 1], 1e-5, None, ALU.add).then_inc(sem("ln2_var"), 1)

            def apply_ln2(u):
                dve.wait_ge(sem("ln2_done"), 3 * (u + 1))
                if u >= 2:
                    dve.wait_ge(sem(f"disp_in{u % 2}"), 16 * T * (u // 2))
                for t in range(T):
                    i = T * u + t
                    ins = V.tensor_scalar(core[:, u % 2, t, 0:D], xs[:, i, :], mv2[:, i, 0:1], cscale[:, i:i + 1],
                                          ALU.subtract, ALU.mult)
                ins.then_inc(sem("core_ready"), 1)
                dve.wait_ge(sem("core_ready"), u + 1)
                for t in range(T):
                    i = T * u + t
                    own(V.tensor_scalar(xs[:, i, :], xs[:, i, :], oneplus[:, i:i + 1], mrs[:, i:i + 1],
                                        ALU.mult, ALU.subtract))

            def xin(n):
                if n < U:
                    apply_ln2(n)
                dve.wait_ge(sem("cT_done"), n + 1)
                if n == 0:
                    dve.wait_ge(sem("vec_ready"), 1)
                if n >= U:
                    e = n - U
                    dve.wait_ge(sem(f"drow_in{e % 2}"), 16 * (e // 2 + 1))
                    if e >= 2:
                        dve.wait_ge(sem("y_out0"), 16 * (e - 1))
                        dve.wait_ge(sem("y_out1"), 16 * (e - 1))
                    V.tensor_copy(rowid[:, e % 2, :], drow[:, e % 2, :, D]).then_inc(sem("rowid_ready"), 1)
                for kc in range(KC):
                    ins = V.tensor_scalar(t32[:, kc, :], mbank[place[("cT", n)]][:, kc * UT:(kc + 1) * UT],
                                          vecT[:, R_NW + kc:R_NW + kc + 1], vecT[:, R_NB + kc:R_NB + kc + 1],
                                          ALU.mult, ALU.add)
                ins.then_inc(sem("ao_t"), 1)
                dve.wait_ge(sem("xin_hi"), n + 1)
                V.tensor_tensor(xin_lo[:, n % 2, :, :], t32[:, :, :], xin_hi[:, n % 2, :, :].bitcast(f32),
                                ALU.subtract).then_inc(sem("xin_lo"), 1)

            def gate(u):
                if u == 0:
                    dve.wait_ge(sem("route_const"), 6)
                dve.wait_ge(sem("lgT_done"), u + 1)
                L3 = mbank[place[("lgT", u)]][:, 0:T * NG].rearrange("p (t g) -> p t g", t=T)
                V.reduce_max(gmax[:, :, 0], L3[:, :, 0:E], AX)
                after(own(V.reduce_max(gmax[:, :, 1], L3[:, :, E:NG], AX)))
                V.tensor_tensor(gd[:, :, 0:E], L3[:, :, 0:E], gmax[:, :, 0:1].broadcast_to([P, T, E]), ALU.subtract)
                V.tensor_tensor(gd[:, :, E:NG], L3[:, :, E:NG], gmax[:, :, 1:2].broadcast_to([P, T, 2]),
                                ALU.subtract).then_inc(sem("gate_read"), 1)
                dve.wait_ge(sem("gate_read"), u + 1)
                after(own(V.scalar_tensor_tensor(out=gkey[:, :, :], in0=gd[:, :, 0:E], scalar=0.0, in1=desc[:, :, :],
                                                 op0=ALU.is_ge, op1=ALU.mult)))
                after(own(V.reduce_max(gkm[:, :], gkey[:, :, :], AX)))
                n = own(V.tensor_tensor(onehot[:, :, :], desc[:, :, :],
                                        gkm[:, :].unsqueeze(2).broadcast_to([P, T, E]), ALU.is_equal))
                V.tensor_copy(before[:, 0, :], running[:, :])
                after(n)
                after(own(V.tensor_tensor(before[:, 1, :], running[:, :], onehot[:, 0, :], ALU.add)))
                V.tensor_tensor(running[:, :], before[:, 1, :], onehot[:, 1, :], ALU.add)\
                    .then_inc(sem("onehot_ready"), 1)
                own(V.tensor_scalar(gbase[:, :], gkm[:, :], -float(CAP), float(E * CAP), ALU.mult, ALU.add))
                dve.wait_ge(sem("gate_exp"), u + 1)
                V.reduce_sum(gsum[:, :, 0], ge[:, :, 0:E], AX)
                after(own(V.reduce_sum(gsum[:, :, 1], ge[:, :, E:NG], AX)))
                after(own(V.reciprocal(grec[:, :, :], gsum[:, :, :])))
                own(V.tensor_tensor(coef0[:, T * u:T * u + T], ge[:, :, E], grec[:, :, 1], ALU.mult))
                after(own(V.tensor_tensor(gw[:, :], ge[:, :, E + 1], grec[:, :, 1], ALU.mult)))
                own(V.tensor_tensor(gw[:, :], gw[:, :], grec[:, :, 0], ALU.mult))

            def place_rows(u):
                dve.wait_ge(sem("loc_done"), u + 1)
                b = mbank[place[("loc", u)]][:, 0:T * E].rearrange("p (t e) -> p t e", t=T)
                V.tensor_tensor(gloc[:, :, :], b, onehot[:, :, :], ALU.mult).then_inc(sem("loc_read"), 1)
                dve.wait_ge(sem("loc_read"), u + 1)
                after(own(V.reduce_sum(gl[:, :], gloc[:, :, :], AX)))
                V.tensor_scalar(gkeep[:, :], gl[:, :], float(CAP), None, ALU.is_lt)
                after(own(V.tensor_tensor(gs0[:, :], gbase[:, :], gl[:, :], ALU.add)))
                beyond = past[:, T * u:T * u + T]
                after(own(V.tensor_tensor(gs0[:, :], gs0[:, :], beyond, ALU.subtract)))
                after(own(V.tensor_tensor(gs1[:, :], gs0[:, :], gkeep[:, :], ALU.mult)))
                V.tensor_tensor(slot[:, T * u:T * u + T], gs1[:, :], beyond, ALU.add)
                V.tensor_copy(core[:, u % 2, :, D], tokid[:, T * u:T * u + T])
                V.tensor_tensor(core[:, u % 2, :, D + 1], gw[:, :], gkeep[:, :], ALU.mult)\
                    .then_inc(sem("slot_ready"), 1)

            def down(n, t):
                dve.wait_ge(sem("down_done"), T * n + t + 1)
                b = mbank[place[("down", n, t)]][:, 0:D]
                if n < U:
                    i = T * n + t
                    if i == 0:
                        dve.wait_ge(sem("resb_in"), 16)
                        after(steps[0])
                    V.tensor_tensor(dtmp[:, t, :], b, resb[:, :], ALU.add).then_inc(sem("down_read"), 1)
                    dve.wait_ge(sem("down_read"), T * n + t + 1)
                    V.scalar_tensor_tensor(out=xs[:, i, :], in0=dtmp[:, t, :], scalar=coef0[:, i:i + 1],
                                           in1=xs[:, i, :], op0=ALU.mult, op1=ALU.add).then_inc(sem("acc_ready"), 1)
                else:
                    e = n - U
                    if t == 0:
                        dve.wait_ge(sem(f"outb_in{e % 2}"), 16 * (e // 2 + 1))
                        dve.wait_ge(sem(f"accg_in{e % 2}"), 16 * T * (e // 2 + 1))
                    V.tensor_tensor(dtmp[:, t, :], b, outb[:, e % 2, :], ALU.add).then_inc(sem("down_read"), 1)
                    dve.wait_ge(sem("down_read"), T * n + t + 1)
                    if e >= 1:
                        dve.wait_ge(sem(f"y_out{t}"), 16 * e)
                    V.scalar_tensor_tensor(out=yrow[:, t, :], in0=dtmp[:, t, :],
                                           scalar=drow[:, e % 2, t, D + 1:ROW], in1=accg[:, e % 2, t, :],
                                           op0=ALU.mult, op1=ALU.add).then_inc(sem("y_ready"), 1)

            def up(n, c2):
                i = (FC // 2) * n + c2
                dve.wait_ge(sem("h_hi"), i + 1)
                V.tensor_tensor(h_lo[:, n % 2, 2 * c2:2 * c2 + 2, :], h32[:, i % 2, :, :],
                                h_hi[:, n % 2, 2 * c2:2 * c2 + 2, :].bitcast(f32), ALU.subtract)\
                    .then_inc(sem("h_lo"), 1)

            calls = {"small": small, "up": up, "ln1": ln1, "xn": norm_x, "tr": tr, "qkv": qkv, "vt": vt, "A": score_max,
                     "M": max_rows, "B": scores_T, "PV": weigh, "oT": oT, "proj": proj, "ln2": ln2, "cT": xin,
                     "ein": lambda e: xin(U + e), "lgT": gate, "loc": place_rows, "down": down}
            for step in plan:
                if step[0] in calls:
                    calls[step[0]](*step[1:])


_INS = ['x', 'ctx_1024', 'L0_xattn_w_q', 'L0_xattn_w_kv', 'L0_xattn_w_concat', 'L0_ffn_attn_nw', 'L0_ffn_attn_nb',
        'L0_ffn_wg', 'L0_ffn_inter_w', 'L0_ffn_inter_b', 'L0_ffn_output_w', 'L0_ffn_output_b', 'L0_ffn_res_inter_w',
        'L0_ffn_res_inter_b', 'L0_ffn_res_output_w', 'L0_ffn_res_output_b', 'L0_ffn_res_coef']


def kernel(**inputs):
    import numpy as _np
    import concourse.bacc as _bacc
    from concourse import mybir as _mybir
    from concourse.bass_utils import run_bass_kernel_spmd as _run

    nc = _bacc.Bacc("TRN2", target_bir_lowering=False, num_devices=1)
    arrays, args = {}, []
    for name in _INS:
        a = _np.ascontiguousarray(inputs[name])
        arrays[f"in_{name}"] = a
        args.append(nc.dram_tensor(f"in_{name}", a.shape, _mybir.dt.from_np(a.dtype), kind="ExternalInput").ap())
    nb, l, d = inputs['x'].shape
    args.append(nc.dram_tensor("out_rows", (nb * l + 512, d), _mybir.dt.float32, kind="ExternalOutput").ap())
    xattn_moe_ffn_kernel(nc, *args)
    r = _run(nc, [arrays], core_ids=[0])
    return r.results[0]["out_rows"][:nb * l].reshape(nb, l, d)
```
